# Optimizing a Trainium2 kernel written in Bass

```python
import numpy as np
import jax
import jax.numpy as jnp

def _softmax(x, axis=-1):
    return jax.nn.softmax(x, axis=axis)

def _gelu(x):
    return jax.nn.gelu(x, approximate=True)

def _silu(x):
    return jax.nn.silu(x)

def _sigmoid(x):
    return jax.nn.sigmoid(x)

def _layernorm(x, axis=-1, eps=1e-05):
    m = jnp.mean(x, axis=axis, keepdims=True)
    v = jnp.var(x, axis=axis, keepdims=True)
    return (x - m) / jnp.sqrt(v + eps)

def _scatter_add(tgt, idx, src, axis=0):
    return tgt.at[idx].add(src)

def _segment_sum(src, seg, n):
    return jax.ops.segment_sum(src, seg, n)
kernel_name = 'mk_dlrm_tower_d1_rec_r8_222794'

def setup_inputs(seed: int=0):
    np.random.seed(seed)
    _w = jnp.asarray

    def _rec_inputs():
        import jax
        import jax.numpy as jnp
        _tk = jax.random.key(seed)
        dense_ctx = jax.random.normal(jax.random.fold_in(_tk, 190), (2048, 16), jnp.float32)
        ids = jnp.stack([jax.random.randint(jax.random.fold_in(_tk, 200 + f), (2048,), 0, v, jnp.int32) for f, v in enumerate([12500, 1250, 1000, 1250, 12500, 12500, 1250, 12500, 1250, 1250, 1250, 12500, 12500, 1250, 1250, 1250, 1250, 12500, 1250, 12500, 1000, 1250, 1000, 1000, 1250, 1000, 1250, 1000, 1000, 1250, 1250, 1000])], axis=1)
        tbl_0 = 0.05 * jax.random.normal(jax.random.fold_in(_tk, 500 + 0), (12500, 256), jnp.float32)
        tbl_1 = 0.05 * jax.random.normal(jax.random.fold_in(_tk, 500 + 1), (1250, 256), jnp.float32)
        tbl_2 = 0.05 * jax.random.normal(jax.random.fold_in(_tk, 500 + 2), (1000, 256), jnp.float32)
        tbl_3 = 0.05 * jax.random.normal(jax.random.fold_in(_tk, 500 + 3), (1250, 256), jnp.float32)
        tbl_4 = 0.05 * jax.random.normal(jax.random.fold_in(_tk, 500 + 4), (12500, 256), jnp.float32)
        tbl_5 = 0.05 * jax.random.normal(jax.random.fold_in(_tk, 500 + 5), (12500, 256), jnp.float32)
        tbl_6 = 0.05 * jax.random.normal(jax.random.fold_in(_tk, 500 + 6), (1250, 256), jnp.float32)
        tbl_7 = 0.05 * jax.random.normal(jax.random.fold_in(_tk, 500 + 7), (12500, 256), jnp.float32)
        tbl_8 = 0.05 * jax.random.normal(jax.random.fold_in(_tk, 500 + 8), (1250, 256), jnp.float32)
        tbl_9 = 0.05 * jax.random.normal(jax.random.fold_in(_tk, 500 + 9), (1250, 256), jnp.float32)
        tbl_10 = 0.05 * jax.random.normal(jax.random.fold_in(_tk, 500 + 10), (1250, 256), jnp.float32)
        tbl_11 = 0.05 * jax.random.normal(jax.random.fold_in(_tk, 500 + 11), (12500, 256), jnp.float32)
        tbl_12 = 0.05 * jax.random.normal(jax.random.fold_in(_tk, 500 + 12), (12500, 256), jnp.float32)
        tbl_13 = 0.05 * jax.random.normal(jax.random.fold_in(_tk, 500 + 13), (1250, 256), jnp.float32)
        tbl_14 = 0.05 * jax.random.normal(jax.random.fold_in(_tk, 500 + 14), (1250, 256), jnp.float32)
        tbl_15 = 0.05 * jax.random.normal(jax.random.fold_in(_tk, 500 + 15), (1250, 256), jnp.float32)
        tbl_16 = 0.05 * jax.random.normal(jax.random.fold_in(_tk, 500 + 16), (1250, 256), jnp.float32)
        tbl_17 = 0.05 * jax.random.normal(jax.random.fold_in(_tk, 500 + 17), (12500, 256), jnp.float32)
        tbl_18 = 0.05 * jax.random.normal(jax.random.fold_in(_tk, 500 + 18), (1250, 256), jnp.float32)
        tbl_19 = 0.05 * jax.random.normal(jax.random.fold_in(_tk, 500 + 19), (12500, 256), jnp.float32)
        tbl_20 = 0.05 * jax.random.normal(jax.random.fold_in(_tk, 500 + 20), (1000, 256), jnp.float32)
        tbl_21 = 0.05 * jax.random.normal(jax.random.fold_in(_tk, 500 + 21), (1250, 256), jnp.float32)
        tbl_22 = 0.05 * jax.random.normal(jax.random.fold_in(_tk, 500 + 22), (1000, 256), jnp.float32)
        tbl_23 = 0.05 * jax.random.normal(jax.random.fold_in(_tk, 500 + 23), (1000, 256), jnp.float32)
        tbl_24 = 0.05 * jax.random.normal(jax.random.fold_in(_tk, 500 + 24), (1250, 256), jnp.float32)
        tbl_25 = 0.05 * jax.random.normal(jax.random.fold_in(_tk, 500 + 25), (1000, 256), jnp.float32)
        tbl_26 = 0.05 * jax.random.normal(jax.random.fold_in(_tk, 500 + 26), (1250, 256), jnp.float32)
        tbl_27 = 0.05 * jax.random.normal(jax.random.fold_in(_tk, 500 + 27), (1000, 256), jnp.float32)
        tbl_28 = 0.05 * jax.random.normal(jax.random.fold_in(_tk, 500 + 28), (1000, 256), jnp.float32)
        tbl_29 = 0.05 * jax.random.normal(jax.random.fold_in(_tk, 500 + 29), (1250, 256), jnp.float32)
        tbl_30 = 0.05 * jax.random.normal(jax.random.fold_in(_tk, 500 + 30), (1250, 256), jnp.float32)
        tbl_31 = 0.05 * jax.random.normal(jax.random.fold_in(_tk, 500 + 31), (1000, 256), jnp.float32)
        _rk = jax.random.fold_in(_tk, 7)
        W_top1 = 0.0441942 * jax.random.normal(jax.random.fold_in(_tk, 801), (512, 512), jnp.float32)
        W_top2 = 0.0441942 * jax.random.normal(jax.random.fold_in(_tk, 802), (512, 256), jnp.float32)
        W_top3 = 0.0625 * jax.random.normal(jax.random.fold_in(_tk, 803), (256, 1), jnp.float32)
        b_top1 = jnp.zeros((512,), jnp.float32)
        b_top2 = jnp.zeros((256,), jnp.float32)
        return (dense_ctx, ids, tbl_0, tbl_1, tbl_2, tbl_3, tbl_4, tbl_5, tbl_6, tbl_7, tbl_8, tbl_9, tbl_10, tbl_11, tbl_12, tbl_13, tbl_14, tbl_15, tbl_16, tbl_17, tbl_18, tbl_19, tbl_20, tbl_21, tbl_22, tbl_23, tbl_24, tbl_25, tbl_26, tbl_27, tbl_28, tbl_29, tbl_30, tbl_31, W_top1, b_top1, W_top2, b_top2, W_top3)
    dense_ctx, ids, tbl_0, tbl_1, tbl_2, tbl_3, tbl_4, tbl_5, tbl_6, tbl_7, tbl_8, tbl_9, tbl_10, tbl_11, tbl_12, tbl_13, tbl_14, tbl_15, tbl_16, tbl_17, tbl_18, tbl_19, tbl_20, tbl_21, tbl_22, tbl_23, tbl_24, tbl_25, tbl_26, tbl_27, tbl_28, tbl_29, tbl_30, tbl_31, W_top1, b_top1, W_top2, b_top2, W_top3 = _rec_inputs()

    def _L0_rec_setup():
        import jax, jax.numpy as jnp
        import numpy as np
        B, N, D = (1024, 32, 256)
        key = jax.random.key(seed)
        x = jax.random.normal(key, (B, N, D), dtype=jnp.float32)
        return {'x': x}
    _L0_rec_all = _L0_rec_setup()
    _L0_rec_in = {k: v for k, v in _L0_rec_all.items() if k in ()}
    del _L0_rec_all
    return {'dense_ctx': dense_ctx, 'ids': ids, 'tbl_0': tbl_0, 'tbl_1': tbl_1, 'tbl_2': tbl_2, 'tbl_3': tbl_3, 'tbl_4': tbl_4, 'tbl_5': tbl_5, 'tbl_6': tbl_6, 'tbl_7': tbl_7, 'tbl_8': tbl_8, 'tbl_9': tbl_9, 'tbl_10': tbl_10, 'tbl_11': tbl_11, 'tbl_12': tbl_12, 'tbl_13': tbl_13, 'tbl_14': tbl_14, 'tbl_15': tbl_15, 'tbl_16': tbl_16, 'tbl_17': tbl_17, 'tbl_18': tbl_18, 'tbl_19': tbl_19, 'tbl_20': tbl_20, 'tbl_21': tbl_21, 'tbl_22': tbl_22, 'tbl_23': tbl_23, 'tbl_24': tbl_24, 'tbl_25': tbl_25, 'tbl_26': tbl_26, 'tbl_27': tbl_27, 'tbl_28': tbl_28, 'tbl_29': tbl_29, 'tbl_30': tbl_30, 'tbl_31': tbl_31, 'W_top1': W_top1, 'b_top1': b_top1, 'W_top2': W_top2, 'b_top2': b_top2, 'W_top3': W_top3}

def reference(dense_ctx, ids, tbl_0, tbl_1, tbl_2, tbl_3, tbl_4, tbl_5, tbl_6, tbl_7, tbl_8, tbl_9, tbl_10, tbl_11, tbl_12, tbl_13, tbl_14, tbl_15, tbl_16, tbl_17, tbl_18, tbl_19, tbl_20, tbl_21, tbl_22, tbl_23, tbl_24, tbl_25, tbl_26, tbl_27, tbl_28, tbl_29, tbl_30, tbl_31, W_top1, b_top1, W_top2, b_top2, W_top3):
    import jax
    import jax.numpy as jnp

    def _L0_rec_ref(x):
        import jax, jax.numpy as jnp
        import numpy as np
        B, N, D = (1024, 32, 256)
        'Second-order feature interaction (DLRM dot interaction).\n\n            Computes dot(x_i, x_j) for all field pairs i < j (self_interaction=False),\n            flattened in row-major upper-triangular order -> [B, N*(N-1)/2].\n            Matches tf.boolean_mask(dot_products, strictly_upper_mask) ordering.\n            '
        b, n, d = x.shape
        iu, ju = jnp.triu_indices(n, k=1)
        dots = jnp.einsum('bnd,bmd->bnm', x, x)
        return dots[:, iu, ju]
    e = jnp.stack([tbl_0[ids[:, 0]], tbl_1[ids[:, 1]], tbl_2[ids[:, 2]], tbl_3[ids[:, 3]], tbl_4[ids[:, 4]], tbl_5[ids[:, 5]], tbl_6[ids[:, 6]], tbl_7[ids[:, 7]], tbl_8[ids[:, 8]], tbl_9[ids[:, 9]], tbl_10[ids[:, 10]], tbl_11[ids[:, 11]], tbl_12[ids[:, 12]], tbl_13[ids[:, 13]], tbl_14[ids[:, 14]], tbl_15[ids[:, 15]], tbl_16[ids[:, 16]], tbl_17[ids[:, 17]], tbl_18[ids[:, 18]], tbl_19[ids[:, 19]], tbl_20[ids[:, 20]], tbl_21[ids[:, 21]], tbl_22[ids[:, 22]], tbl_23[ids[:, 23]], tbl_24[ids[:, 24]], tbl_25[ids[:, 25]], tbl_26[ids[:, 26]], tbl_27[ids[:, 27]], tbl_28[ids[:, 28]], tbl_29[ids[:, 29]], tbl_30[ids[:, 30]], tbl_31[ids[:, 31]]], axis=1)
    z = _L0_rec_ref(e)
    z = z.reshape(z.shape[0], -1)
    h = jnp.concatenate([z, dense_ctx], axis=1)
    h = jnp.maximum(h @ W_top1 + b_top1, 0.0)
    h = jnp.maximum(h @ W_top2 + b_top2, 0.0)
    y = h @ W_top3
    return y

_drawn_inputs = setup_inputs


def setup_inputs(seed=0):
    import zlib

    import numpy as np

    out = dict(_drawn_inputs(seed))
    spreads = {'b_top1': (0.0, 0.1), 'b_top2': (0.0, 0.1)}
    factors = {}
    for name, (base, spread) in spreads.items():
        noise = np.random.default_rng([zlib.crc32(name.encode()), seed]).standard_normal(out[name].shape)
        drawn = base * np.exp(spread * noise) if base else spread * noise
        out[name] = jnp.asarray(drawn.astype(out[name].dtype))
    for name, factor in factors.items():
        out[name] = (out[name] * factor).astype(out[name].dtype)
    return out
```

```python
from contextlib import ExitStack

import concourse.bass as bass
from concourse import mybir

ALU = mybir.AluOpType
ACT = mybir.ActivationFunctionType
F32 = mybir.dt.float32
I32 = mybir.dt.int32

P = 128
Q = 32
NF = 32
GB = P // NF
PAIR = 2
STEP = 8
XT_SLOTS = 4
NJ = NF // (P // Q)


def dlrm_tower(
    nc: bass.Bass,
    tables: bass.AP,
    idx: bass.AP,
    table_base: bass.AP,
    dense_t: bass.AP,
    w1: bass.AP,
    w2: bass.AP,
    b2: bass.AP,
    w3: bass.AP,
    out: bass.AP,
):
    D = tables.shape[1]
    NG = idx.shape[1]
    DENSE, B = dense_t.shape
    H1 = w1.shape[2]
    H2 = w2.shape[1]
    DH = D // P
    KH = H1 // P
    TG = P // GB
    TP = TG // PAIR
    TS = TG // STEP
    SP = STEP // PAIR
    NT = B // P
    PC = PAIR * P
    assert DH == 2 and NJ * (P // Q) == NF and DENSE < Q and DH * PC == 512 and NG == NT * TG

    with ExitStack() as ctx:
        def sb(name, shape, dt=F32):
            return ctx.enter_context(nc.sbuf_tensor(name, shape, dt))

        def psum(name, shape):
            return ctx.enter_context(nc.psum_tensor(name, shape, F32))

        def sem(name):
            return ctx.enter_context(nc.semaphore(name))

        ids = sb("ids", [P, NG], I32)
        base = sb("base", [P, 1], I32)
        rows = sb("rows", [P, NG + TG // 2], I32)
        tile_rows = sb("tile_rows", [P, TG], I32)
        emb = sb("emb", [P, TG, D])
        emb_t = sb("emb_t", [P, XT_SLOTS, DH, PC])
        dots = sb("dots", [P, NJ, P])
        ident = sb("ident", [P, P])
        w1_sb = sb("w1_sb", [P, NJ, H1])
        w2_sb = sb("w2_sb", [P, KH, H2])
        b2_sb = sb("b2_sb", [P, H2])
        w3_sb = sb("w3_sb", [P, H2])
        h1 = sb("h1", [P, H1])
        h1_t = sb("h1_t", [P, KH, P])
        h2 = sb("h2", [P, H2])
        h2w = sb("h2w", [P, H2])
        y = sb("y", [P, NT])
        y_t = sb("y_t", [NT, P])

        tr_ps = psum("tr_ps", [P, 2, DH, PC])
        gram_ps = psum("gram_ps", [P, 2, STEP, P])
        mlp_ps = psum("mlp_ps", [P, 512])
        ht_ps = psum("ht_ps", [P, KH, P])

        ids_loaded = sem("ids_loaded")
        consts_loaded = sem("consts_loaded")
        rows_ready = sem("rows_ready")
        tile_rows_low = sem("tile_rows_low")
        tile_rows_high = sem("tile_rows_high")
        steps_opened = sem("steps_opened")
        ident_zeroed = sem("ident_zeroed")
        ident_ready = sem("ident_ready")
        ones_ready = sem("ones_ready")
        gathered = [sem(f"gathered{p}") for p in range(TP)]
        transposed = sem("transposed")
        copied_even = sem("copied_even")
        copied_odd = sem("copied_odd")
        multiplied = sem("multiplied")
        dots_low = sem("dots_low")
        dots_high = sem("dots_high")
        dense_loaded = sem("dense_loaded")
        layer1_done = sem("layer1_done")
        h1_ready = sem("h1_ready")
        h1_transposed = sem("h1_transposed")
        h1_t_ready = sem("h1_t_ready")
        layer2_done = sem("layer2_done")
        mlp_ps_free = sem("mlp_ps_free")
        y_ready = sem("y_ready")
        y_transposed = sem("y_transposed")
        y_t_ready = sem("y_t_ready")
        out_stored = sem("out_stored")

        block = ctx.enter_context(nc.Block())

        def dots_of_quadrant(copy, s, q):
            for jj in range(P // Q):
                lo = 1 if jj == 0 else 0
                src = gram_ps[Q * q:Q * q + Q, s % 2, :, Q * q + NJ * jj + lo:Q * q + NJ * jj + NJ]
                dst = dots[Q * jj:Q * jj + Q, lo:NJ, GB * STEP * s + q:GB * STEP * (s + 1):GB]
                last = copy(dst, src.rearrange("p g j -> p j g"))
            return last

        @block.sync
        def _(sp):
            sp.dma_start(ids[:, :], idx).then_inc(ids_loaded, 16)
            sp.dma_start(base[:, :], table_base).then_inc(ids_loaded, 16)
            sp.dma_start(w1_sb[:, :, :], w1).then_inc(consts_loaded, 16)
            sp.dma_start(w2_sb[:, :, :], w2.rearrange("(k p) n -> p k n", p=P)).then_inc(consts_loaded, 16)
            sp.dma_start(b2_sb[:, :], b2.broadcast_to([P, H2])).then_inc(consts_loaded, 16)
            sp.dma_start(w3_sb[:, :], w3.broadcast_to([P, H2])).then_inc(consts_loaded, 16)
            sp.wait_ge(ones_ready, 1)
            sp.dma_start(dots[0:DENSE, 0, :], dense_t[:, 0:P]).then_inc(dense_loaded, 16)
            with sp.Fori(1, NT) as t:
                sp.wait_ge(layer1_done, t)
                sp.dma_start(dots[0:DENSE, 0, :], dense_t[:, bass.ds(t * P, P)]).then_inc(dense_loaded, 16)
            sp.wait_ge(y_t_ready, 1)
            sp.dma_start(out, y_t[:, :]).then_inc(out_stored, 16)
            sp.wait_ge(out_stored, 16)

        @block.gpsimd
        def _(pool):
            pool.wait_ge(ids_loaded, 32)
            nc.gpsimd.tensor_tensor(rows[:, 0:NG], ids[:, :], base[:, 0:1].broadcast_to([P, NG]),
                                    ALU.add).then_inc(rows_ready, 1)
            nc.gpsimd.memset(rows[:, NG:], 0).then_inc(rows_ready, 1)
            nc.gpsimd.memset(ident[:, :], 0.0).then_inc(ident_zeroed, 1)
            pool.wait_ge(ident_zeroed, 1)
            nc.gpsimd.affine_select(out=ident[:, :], in_=ident[:, :], compare_op=ALU.not_equal, fill=1.0,
                                    base=0, pattern=[[-1, P]], channel_multiplier=1).then_inc(ident_ready, 1)

            def gather_tile(t, first):
                for k in range(TG):
                    if k % STEP == 0:
                        if k == 0:
                            pool.wait_ge(tile_rows_low, t + 1)
                        if k == TG // 2:
                            pool.wait_ge(tile_rows_high, t + 1)
                        if not first:
                            pool.wait_ge(transposed, t * TP - TP + (k + STEP) // PAIR)
                        pool.sem_inc(steps_opened, 1)
                    nc.gpsimd.indirect_dma_start(
                        out=emb[:, k, :], out_offset=None, in_=tables,
                        in_offset=bass.IndirectOffsetOnAxis(ap=tile_rows[:, k:k + 1], axis=0),
                    ).then_inc(gathered[k // PAIR], 16)

            gather_tile(0, True)
            with pool.Fori(1, NT) as t:
                gather_tile(t, False)

        @block.tensor
        def _(pe):
            def transpose_pair(t, p, first):
                pe.wait_ge(gathered[p], (t + 1) * (16 * PAIR))
                if p >= 2 or not first:
                    pe.wait_ge(copied_odd if p % 2 else copied_even, t * (TP // 2) + p // 2)
                for h in range(DH):
                    for a in range(PAIR):
                        last = nc.tensor.transpose(tr_ps[:, p % 2, h, a * P:(a + 1) * P],
                                                   emb[:, p * PAIR + a, h * P:(h + 1) * P], ident[:, :])
                last.then_inc(transposed, 1)

            def multiply_pair(t, p, first):
                s = p // SP
                if p % SP == 0 and (s >= 2 or not first):
                    pe.wait_ge(dots_low, t * TS + s - 1)
                    pe.wait_ge(dots_high, t * TS + s - 1)
                pe.wait_ge(copied_odd if p % 2 else copied_even, t * (TP // 2) + p // 2 + 1)
                for a in range(PAIR):
                    for h in range(DH):
                        x = emb_t[:, p % XT_SLOTS, h, a * P:(a + 1) * P]
                        last = nc.tensor.matmul(gram_ps[:, s % 2, (p % SP) * PAIR + a, :], x, x,
                                                start=(h == 0), stop=(h == DH - 1))
                last.then_inc(multiplied, 1)

            def layer1(t):
                pe.wait_ge(dots_low, (t + 1) * TS)
                pe.wait_ge(dots_high, (t + 1) * TS)
                pe.wait_ge(dense_loaded, (t + 1) * 16)
                pe.wait_ge(mlp_ps_free, t + 1)
                for j in range(NJ):
                    last = nc.tensor.matmul(mlp_ps[:, 0:H1], dots[:, j, :], w1_sb[:, j, :],
                                            start=(j == 0), stop=(j == NJ - 1))
                last.then_inc(layer1_done, 1)

            def transpose_h1(t):
                pe.wait_ge(h1_ready, t + 1)
                for k in range(KH):
                    last = nc.tensor.transpose(ht_ps[:, k, :], h1[:, k * P:(k + 1) * P], ident[:, :])
                last.then_inc(h1_transposed, 1)

            def layer2(t):
                pe.wait_ge(h1_t_ready, t + 1)
                for k in range(KH):
                    last = nc.tensor.matmul(mlp_ps[:, 0:H2], h1_t[:, k, :], w2_sb[:, k, :],
                                            start=(k == 0), stop=(k == KH - 1))
                last.then_inc(layer2_done, 1)

            def tile(t, first):
                for p in range(TP):
                    transpose_pair(t, p, first)
                    if p > 0:
                        multiply_pair(t, p - 1, first)
                    elif not first:
                        multiply_pair(t - 1, TP - 1, False)
                    if not first and p == SP:
                        layer1(t - 1)
                    if not first and p == SP + 2:
                        transpose_h1(t - 1)
                    if not first and p == SP + 4:
                        layer2(t - 1)

            pe.wait_ge(ident_ready, 1)
            tile(0, True)
            pe.wait_ge(consts_loaded, 64)
            with pe.Fori(1, NT) as t:
                tile(t, False)
            multiply_pair(NT - 1, TP - 1, False)
            layer1(NT - 1)
            transpose_h1(NT - 1)
            layer2(NT - 1)
            pe.wait_ge(y_ready, NT)
            nc.tensor.transpose(ht_ps[0:NT, 0, :], y[:, :], ident[:, :]).then_inc(y_transposed, 1)

        @block.vector
        def _(dve):
            def copy_pair(t, p, first):
                dve.wait_ge(transposed, t * TP + p + 1)
                if p >= XT_SLOTS or not first:
                    dve.wait_ge(multiplied, t * TP + p - XT_SLOTS + 1)
                nc.vector.tensor_copy(emb_t[:, p % XT_SLOTS, :, :], tr_ps[:, p % 2, :, :]).then_inc(copied_even, 1)

            def place_rows(t, half):
                lo = half * TG // 2
                nc.vector.tensor_copy(tile_rows[:, lo:lo + TG // 2], rows[:, bass.ds(t * TG + lo, TG // 2)]).then_inc(
                    tile_rows_high if half else tile_rows_low, 1)

            def copy_dots(t, s, q, first):
                if q == 0:
                    dve.wait_ge(multiplied, t * TP + (s + 1) * SP)
                    if s == 0 and not first:
                        dve.wait_ge(layer1_done, t)
                last = dots_of_quadrant(nc.vector.tensor_copy, s, q)
                if q == 1:
                    last.then_inc(dots_low, 1)

            def copy_h1_t(t):
                dve.wait_ge(h1_transposed, t + 1)
                nc.vector.tensor_copy(h1_t[:, :, :], ht_ps[:, :, :]).then_inc(h1_t_ready, 1)

            def layer3(t):
                dve.wait_ge(layer2_done, t + 1)
                nc.vector.tensor_tensor(h2[:, :], mlp_ps[:, 0:H2], b2_sb[:, :], ALU.add).then_inc(mlp_ps_free, 1)
                dve.wait_ge(mlp_ps_free, t + 2)
                nc.vector.scalar_tensor_tensor(out=h2w[:, :], in0=h2[:, :], scalar=0.0, in1=w3_sb[:, :],
                                               op0=ALU.max, op1=ALU.mult,
                                               accum_out=y[:, bass.ds(t, 1)]).then_inc(y_ready, 1)

            def tile(t, first):
                for p in range(0, TP, 2):
                    copy_pair(t, p, first)
                    if p == 0 and not first:
                        place_rows(t, 1)
                    if p == TP // 2:
                        place_rows(t + 1, 0)
                    s, q = p // SP - 1, p % SP // 2
                    if s >= 0:
                        copy_dots(t, s, q, first)
                    elif not first:
                        copy_dots(t - 1, TS - 1, q, False)
                    if not first and p == SP + 2:
                        copy_h1_t(t - 1)
                    if not first and p == SP + 4:
                        layer3(t - 1)

            dve.sem_inc(mlp_ps_free, 1)
            nc.vector.memset(dots[0:Q, 0, :], 1.0).then_inc(ones_ready, 1)
            dve.wait_ge(rows_ready, 2)
            place_rows(0, 0)
            place_rows(0, 1)
            tile(0, True)
            dve.wait_ge(consts_loaded, 64)
            with dve.Fori(1, NT) as t:
                tile(t, False)
            copy_dots(NT - 1, TS - 1, 0, False)
            copy_dots(NT - 1, TS - 1, 1, False)
            copy_h1_t(NT - 1)
            layer3(NT - 1)
            dve.wait_ge(y_transposed, 1)
            nc.vector.tensor_copy(y_t[:, :], ht_ps[0:NT, 0, :]).then_inc(y_t_ready, 1)

        @block.scalar
        def _(act):
            def copy_pair(t, p, first):
                act.wait_ge(transposed, t * TP + p + 1)
                if p >= XT_SLOTS or not first:
                    act.wait_ge(multiplied, t * TP + p - XT_SLOTS + 1)
                nc.scalar.copy(emb_t[:, p % XT_SLOTS, :, :], tr_ps[:, p % 2, :, :]).then_inc(copied_odd, 1)

            def copy_dots(t, s, q, first):
                if q == 2:
                    act.wait_ge(multiplied, t * TP + (s + 1) * SP)
                    if s == 0 and not first:
                        act.wait_ge(layer1_done, t)
                last = dots_of_quadrant(nc.scalar.copy, s, q)
                if q == 3:
                    last.then_inc(dots_high, 1)

            def relu_h1(t):
                act.wait_ge(layer1_done, t + 1)
                nc.scalar.activation(h1[:, :], mlp_ps[:, 0:H1], ACT.Relu).then_inc(h1_ready, 1)

            def tile(t, first):
                for p in range(1, TP, 2):
                    if not first and p == SP + 1:
                        relu_h1(t - 1)
                    copy_pair(t, p, first)
                    s, q = p // SP - 1, 2 + p % SP // 2
                    if s >= 0:
                        copy_dots(t, s, q, first)
                    elif not first:
                        copy_dots(t - 1, TS - 1, q, False)

            tile(0, True)
            with act.Fori(1, NT) as t:
                tile(t, False)
            copy_dots(NT - 1, TS - 1, 2, False)
            copy_dots(NT - 1, TS - 1, 3, False)
            relu_h1(NT - 1)


def kernel(**inputs):
    import numpy as np
    import concourse.bacc as bacc
    from concourse import mybir as mb
    from concourse.bass_utils import run_bass_kernel_spmd as run

    tbls = [np.asarray(inputs[f"tbl_{f}"]) for f in range(NF)]
    ids = np.asarray(inputs["ids"])
    w1 = np.asarray(inputs["W_top1"])
    b = ids.shape[0]
    h1 = w1.shape[1]

    starts = np.cumsum([0] + [t.shape[0] for t in tbls])[:NF].astype(np.int32)

    w1_l = np.zeros((P // Q, Q, NJ, h1), w1.dtype)
    iu, ju = np.triu_indices(NF, k=1)
    w1_l[ju // NJ, iu, ju % NJ] = w1[:iu.size]
    dense = w1.shape[0] - iu.size
    w1_l[0, :dense, 0] = w1[iu.size:]
    w1_l[0, dense, 0] = np.asarray(inputs["b_top1"])

    arrays = {
        "tables": np.concatenate(tbls, axis=0),
        "idx": np.ascontiguousarray(ids.reshape(b // GB, GB * NF).T),
        "table_base": np.tile(starts, GB).reshape(P, 1),
        "dense_t": np.ascontiguousarray(np.asarray(inputs["dense_ctx"]).T),
        "w1": w1_l.reshape(P, NJ, h1),
        "w2": np.asarray(inputs["W_top2"]),
        "b2": np.asarray(inputs["b_top2"]).reshape(1, -1),
        "w3": np.asarray(inputs["W_top3"]).reshape(1, -1),
    }
    nc = bacc.Bacc("TRN2", target_bir_lowering=False, num_devices=1)
    args = [nc.dram_tensor(n, a.shape, mb.dt.from_np(a.dtype), kind="ExternalInput").ap()
            for n, a in arrays.items()]
    out = nc.dram_tensor("out", (b // P, P), mb.dt.float32, kind="ExternalOutput").ap()
    dlrm_tower(nc, *args, out)
    r = run(nc, [arrays], core_ids=[0])
    return r.results[0]["out"].reshape(b, 1)
```

```python
from contextlib import ExitStack

import concourse.bass as bass
from concourse import mybir

ALU = mybir.AluOpType
ACT = mybir.ActivationFunctionType
F32 = mybir.dt.float32
I32 = mybir.dt.int32

P = 128
Q = 32
NF = 32
GB = P // NF
PAIR = 2
STEP = 8
XT_SLOTS = 4
NJ = NF // (P // Q)


def dlrm_tower(
    nc: bass.Bass,
    tables: bass.AP,
    idx: bass.AP,
    table_base: bass.AP,
    dense_t: bass.AP,
    w1: bass.AP,
    w2: bass.AP,
    b2: bass.AP,
    w3: bass.AP,
    out: bass.AP,
):
    D = tables.shape[1]
    NG = idx.shape[1]
    DENSE, B = dense_t.shape
    H1 = w1.shape[2]
    H2 = w2.shape[1]
    DH = D // P
    KH = H1 // P
    TG = P // GB
    TP = TG // PAIR
    TS = TG // STEP
    SP = STEP // PAIR
    NT = B // P
    PC = PAIR * P
    assert DH == 2 and NJ * (P // Q) == NF and DENSE < Q and DH * PC == 512 and NG == NT * TG

    with ExitStack() as ctx:
        def sb(name, shape, dt=F32):
            return ctx.enter_context(nc.sbuf_tensor(name, shape, dt))

        def psum(name, shape):
            return ctx.enter_context(nc.psum_tensor(name, shape, F32))

        def sem(name):
            return ctx.enter_context(nc.semaphore(name))

        ids = sb("ids", [P, NG + TG // 2], I32)
        base = sb("base", [P, 1], I32)
        rows = sb("rows", [P, TG], I32)
        emb = sb("emb", [P, TG, D])
        emb_t = sb("emb_t", [P, XT_SLOTS, DH, PC])
        dots = sb("dots", [P, NJ, P])
        ident = sb("ident", [P, P])
        w1_sb = sb("w1_sb", [P, NJ, H1])
        w2_sb = sb("w2_sb", [P, KH, H2])
        b2_sb = sb("b2_sb", [P, H2])
        w3_sb = sb("w3_sb", [P, H2])
        h1 = sb("h1", [P, H1])
        h1_t = sb("h1_t", [P, KH, P])
        h2 = sb("h2", [P, H2])
        h2w = sb("h2w", [P, H2])
        y = sb("y", [P, NT])
        one_row = sb("one_row", [1, P])

        tr_ps = psum("tr_ps", [P, 2, DH, PC])
        gram_ps = psum("gram_ps", [P, 2, STEP, P])
        mlp_ps = psum("mlp_ps", [P, 512])
        ht_ps = psum("ht_ps", [P, KH, P])

        base_loaded = sem("base_loaded")
        first_ids_loaded = sem("first_ids_loaded")
        ids_loaded = sem("ids_loaded")
        ids_padded = sem("ids_padded")
        consts_loaded = sem("consts_loaded")
        rows_low = sem("rows_low")
        rows_high = sem("rows_high")
        steps_opened = sem("steps_opened")
        ident_zeroed = sem("ident_zeroed")
        ident_ready = sem("ident_ready")
        ones_ready = sem("ones_ready")
        one_row_ready = sem("one_row_ready")
        gathered = [sem(f"gathered{p}") for p in range(TP)]
        transposed = sem("transposed")
        copied_even = sem("copied_even")
        copied_odd = sem("copied_odd")
        multiplied = sem("multiplied")
        dots_low = sem("dots_low")
        dots_high = sem("dots_high")
        dense_loaded = sem("dense_loaded")
        layer1_done = sem("layer1_done")
        h1_ready = sem("h1_ready")
        h1_transposed = sem("h1_transposed")
        h1_t_ready = sem("h1_t_ready")
        layer2_done = sem("layer2_done")
        half1_done = sem("half1_done")
        half_h1_ready = sem("half_h1_ready")
        half_transposed = sem("half_transposed")
        half_h1_t_ready = sem("half_h1_t_ready")
        mlp_ps_free = sem("mlp_ps_free")
        y_ready = sem("y_ready")
        out_stored = sem("out_stored")

        KHH = KH // 2
        half_ps = [mlp_ps[:, 0:H1 // 2], tr_ps[:, 0, 0, :]]
        half_t_ps = [ht_ps[:, 0:KHH, :], tr_ps[:, 1, 0, :].rearrange("p (k b) -> p k b", k=KHH)]
        assert PC == H1 // 2

        block = ctx.enter_context(nc.Block())

        def dots_of_quadrant(copy, s, q):
            for jj in range(P // Q):
                lo = 1 if jj == 0 else 0
                src = gram_ps[Q * q:Q * q + Q, s % 2, :, Q * q + NJ * jj + lo:Q * q + NJ * jj + NJ]
                dst = dots[Q * jj:Q * jj + Q, lo:NJ, GB * STEP * s + q:GB * STEP * (s + 1):GB]
                last = copy(dst, src.rearrange("p g j -> p j g"))
            return last

        @block.sync
        def _(sp):
            sp.dma_start(ids[:, 0:TG], idx[:, 0:TG]).then_inc(first_ids_loaded, 16)
            sp.dma_start(ids[:, TG:NG], idx[:, TG:NG]).then_inc(ids_loaded, 16)
            sp.dma_start(w1_sb[:, :, :], w1).then_inc(consts_loaded, 16)
            sp.dma_start(w2_sb[:, :, :], w2.rearrange("(k p) n -> p k n", p=P)).then_inc(consts_loaded, 16)
            sp.dma_start(b2_sb[:, :], b2.broadcast_to([P, H2])).then_inc(consts_loaded, 16)
            sp.dma_start(w3_sb[:, :], w3.broadcast_to([P, H2])).then_inc(consts_loaded, 16)
            sp.wait_ge(ones_ready, 1)
            sp.dma_start(dots[0:DENSE, 0, :], dense_t[:, 0:P]).then_inc(dense_loaded, 16)
            with sp.Fori(1, NT) as t:
                sp.wait_ge(layer1_done, t)
                sp.dma_start(dots[0:DENSE, 0, :], dense_t[:, bass.ds(t * P, P)]).then_inc(dense_loaded, 16)
                sp.wait_ge(y_ready, t)
                sp.dma_start(out[bass.ds(t * P - P, P), :], y[:, bass.ds(t - 1, 1)]).then_inc(out_stored, 16)
            sp.wait_ge(y_ready, NT)
            sp.dma_start(out[B - P:B, :], y[:, NT - 1:NT]).then_inc(out_stored, 16)
            sp.wait_ge(out_stored, 16 * NT)

        @block.gpsimd
        def _(pool):
            nc.gpsimd.memset(ident[:, :], 0.0).then_inc(ident_zeroed, 1)
            pool.wait_ge(ident_zeroed, 1)
            nc.gpsimd.affine_select(out=ident[:, :], in_=ident[:, :], compare_op=ALU.not_equal, fill=1.0,
                                    base=0, pattern=[[-1, P]], channel_multiplier=1).then_inc(ident_ready, 1)

            def gather_tile(t, first):
                for k in range(TG):
                    if k % STEP == 0:
                        if k == 0:
                            pool.wait_ge(rows_low, t + 1)
                        if k == TG // 2:
                            pool.wait_ge(rows_high, t + 1)
                        if not first:
                            pool.wait_ge(transposed, t * TP - TP + (k + STEP) // PAIR)
                        pool.sem_inc(steps_opened, 1)
                    nc.gpsimd.indirect_dma_start(
                        out=emb[:, k, :], out_offset=None, in_=tables,
                        in_offset=bass.IndirectOffsetOnAxis(ap=rows[:, k:k + 1], axis=0),
                    ).then_inc(gathered[k // PAIR], 16)

            gather_tile(0, True)
            with pool.Fori(1, NT) as t:
                gather_tile(t, False)

        @block.tensor
        def _(pe):
            def transpose_pair(t, p, first):
                pe.wait_ge(gathered[p], (t + 1) * (16 * PAIR))
                if p >= 2 or not first:
                    pe.wait_ge(copied_odd if p % 2 else copied_even, t * (TP // 2) + p // 2)
                for h in range(DH):
                    for a in range(PAIR):
                        last = nc.tensor.transpose(tr_ps[:, p % 2, h, a * P:(a + 1) * P],
                                                   emb[:, p * PAIR + a, h * P:(h + 1) * P], ident[:, :])
                last.then_inc(transposed, 1)

            def multiply_pair(t, p, first):
                s = p // SP
                if p % SP == 0 and (s >= 2 or not first):
                    pe.wait_ge(dots_low, t * TS + s - 1)
                    pe.wait_ge(dots_high, t * TS + s - 1)
                pe.wait_ge(copied_odd if p % 2 else copied_even, t * (TP // 2) + p // 2 + 1)
                for a in range(PAIR):
                    for h in range(DH):
                        x = emb_t[:, p % XT_SLOTS, h, a * P:(a + 1) * P]
                        last = nc.tensor.matmul(gram_ps[:, s % 2, (p % SP) * PAIR + a, :], x, x,
                                                start=(h == 0), stop=(h == DH - 1))
                last.then_inc(multiplied, 1)

            def layer1(t):
                pe.wait_ge(dots_low, (t + 1) * TS)
                pe.wait_ge(dots_high, (t + 1) * TS)
                pe.wait_ge(dense_loaded, (t + 1) * 16)
                pe.wait_ge(mlp_ps_free, t + 1)
                for j in range(NJ):
                    last = nc.tensor.matmul(mlp_ps[:, 0:H1], dots[:, j, :], w1_sb[:, j, :],
                                            start=(j == 0), stop=(j == NJ - 1))
                last.then_inc(layer1_done, 1)

            def transpose_h1(t):
                pe.wait_ge(h1_ready, t + 1)
                for k in range(KH):
                    last = nc.tensor.transpose(ht_ps[:, k, :], h1[:, k * P:(k + 1) * P], ident[:, :])
                last.then_inc(h1_transposed, 1)

            def layer2(t):
                pe.wait_ge(h1_t_ready, t + 1)
                for k in range(KH):
                    last = nc.tensor.matmul(mlp_ps[:, 0:H2], h1_t[:, k, :], w2_sb[:, k, :],
                                            start=(k == 0), stop=(k == KH - 1))
                last.then_inc(layer2_done, 1)

            def last_mlp():
                pe.wait_ge(dots_low, NT * TS)
                pe.wait_ge(dots_high, NT * TS)
                pe.wait_ge(dense_loaded, NT * 16)
                pe.wait_ge(mlp_ps_free, NT)
                for c in range(2):
                    for j in range(NJ):
                        last = nc.tensor.matmul(half_ps[c], dots[:, j, :], w1_sb[:, j, c * H1 // 2:(c + 1) * H1 // 2],
                                                start=(j == 0), stop=(j == NJ - 1))
                    last.then_inc(half1_done, 1)
                for c in range(2):
                    pe.wait_ge(half_h1_ready, c + 1)
                    for k in range(KHH):
                        last = nc.tensor.transpose(half_t_ps[c][:, k, :],
                                                   h1[:, (c * KHH + k) * P:(c * KHH + k + 1) * P], ident[:, :])
                    last.then_inc(half_transposed, 1)
                pe.wait_ge(one_row_ready, 1)
                nc.tensor.matmul(mlp_ps[:, 0:H2], one_row[0:1, :], b2_sb[0:1, :], start=True, stop=False)
                for k in range(KH):
                    if k % KHH == 0:
                        pe.wait_ge(half_h1_t_ready, k // KHH + 1)
                    last = nc.tensor.matmul(mlp_ps[:, 0:H2], h1_t[:, k, :], w2_sb[:, k, :],
                                            start=False, stop=(k == KH - 1))
                last.then_inc(layer2_done, 1)

            def tile(t, first):
                for p in range(TP):
                    transpose_pair(t, p, first)
                    if p > 0:
                        multiply_pair(t, p - 1, first)
                    elif not first:
                        multiply_pair(t - 1, TP - 1, False)
                    if not first and p == SP:
                        layer1(t - 1)
                    if not first and p == SP + 2:
                        transpose_h1(t - 1)
                    if not first and p == SP + 4:
                        layer2(t - 1)

            pe.wait_ge(ident_ready, 1)
            tile(0, True)
            pe.wait_ge(consts_loaded, 64)
            with pe.Fori(1, NT) as t:
                tile(t, False)
            multiply_pair(NT - 1, TP - 1, False)
            last_mlp()

        @block.vector
        def _(dve):
            def copy_pair(t, p, first):
                dve.wait_ge(transposed, t * TP + p + 1)
                if p >= XT_SLOTS or not first:
                    dve.wait_ge(multiplied, t * TP + p - XT_SLOTS + 1)
                nc.vector.tensor_copy(emb_t[:, p % XT_SLOTS, :, :], tr_ps[:, p % 2, :, :]).then_inc(copied_even, 1)

            def place_rows(t, half):
                lo = half * TG // 2
                nc.vector.tensor_scalar(rows[:, lo:lo + TG // 2], ids[:, bass.ds(t * TG + lo, TG // 2)], base[:, 0:1],
                                        None, ALU.add).then_inc(rows_high if half else rows_low, 1)

            def copy_dots(t, s, q, first):
                if q == 0:
                    dve.wait_ge(multiplied, t * TP + (s + 1) * SP)
                    if s == 0 and not first:
                        dve.wait_ge(layer1_done, t)
                last = dots_of_quadrant(nc.vector.tensor_copy, s, q)
                if q == 1:
                    last.then_inc(dots_low, 1)

            def copy_h1_t(t):
                dve.wait_ge(h1_transposed, t + 1)
                nc.vector.tensor_copy(h1_t[:, :, :], ht_ps[:, :, :]).then_inc(h1_t_ready, 1)

            def layer3(t):
                dve.wait_ge(layer2_done, t + 1)
                nc.vector.tensor_tensor(h2[:, :], mlp_ps[:, 0:H2], b2_sb[:, :], ALU.add).then_inc(mlp_ps_free, 1)
                dve.wait_ge(mlp_ps_free, t + 2)
                nc.vector.scalar_tensor_tensor(out=h2w[:, :], in0=h2[:, :], scalar=0.0, in1=w3_sb[:, :],
                                               op0=ALU.max, op1=ALU.mult,
                                               accum_out=y[:, bass.ds(t, 1)]).then_inc(y_ready, 1)

            def tile(t, first):
                for p in range(0, TP, 2):
                    copy_pair(t, p, first)
                    if p == 0 and not first:
                        place_rows(t, 1)
                    if p == TP // 2:
                        place_rows(t + 1, 0)
                    s, q = p // SP - 1, p % SP // 2
                    if s >= 0:
                        copy_dots(t, s, q, first)
                    elif not first:
                        copy_dots(t - 1, TS - 1, q, False)
                    if not first and p == SP + 2:
                        copy_h1_t(t - 1)
                    if not first and p == SP + 4:
                        layer3(t - 1)

            dve.sem_inc(mlp_ps_free, 1)
            nc.vector.memset(dots[0:Q, 0, :], 1.0).then_inc(ones_ready, 1)
            nc.vector.memset(one_row[:, :], 1.0).then_inc(one_row_ready, 1)
            nc.vector.memset(ids[:, NG:], 0).then_inc(ids_padded, 1)
            dve.wait_ge(base_loaded, 16)
            dve.wait_ge(first_ids_loaded, 16)
            place_rows(0, 0)
            place_rows(0, 1)
            dve.wait_ge(ids_loaded, 16)
            dve.wait_ge(ids_padded, 1)
            tile(0, True)
            dve.wait_ge(consts_loaded, 64)
            with dve.Fori(1, NT) as t:
                tile(t, False)
            copy_dots(NT - 1, TS - 1, 0, False)
            copy_dots(NT - 1, TS - 1, 1, False)
            for c in range(2):
                dve.wait_ge(half_transposed, c + 1)
                nc.vector.tensor_copy(h1_t[:, c * KHH:(c + 1) * KHH, :], half_t_ps[c]).then_inc(half_h1_t_ready, 1)
            dve.wait_ge(layer2_done, NT)
            nc.vector.scalar_tensor_tensor(out=h2w[:, :], in0=mlp_ps[:, 0:H2], scalar=0.0, in1=w3_sb[:, :],
                                           op0=ALU.max, op1=ALU.mult, accum_out=y[:, NT - 1:NT]).then_inc(y_ready, 1)

        @block.scalar
        def _(act):
            def copy_pair(t, p, first):
                act.wait_ge(transposed, t * TP + p + 1)
                if p >= XT_SLOTS or not first:
                    act.wait_ge(multiplied, t * TP + p - XT_SLOTS + 1)
                nc.scalar.copy(emb_t[:, p % XT_SLOTS, :, :], tr_ps[:, p % 2, :, :]).then_inc(copied_odd, 1)

            def copy_dots(t, s, q, first):
                if q == 2:
                    act.wait_ge(multiplied, t * TP + (s + 1) * SP)
                    if s == 0 and not first:
                        act.wait_ge(layer1_done, t)
                last = dots_of_quadrant(nc.scalar.copy, s, q)
                if q == 3:
                    last.then_inc(dots_high, 1)

            def relu_h1(t):
                act.wait_ge(layer1_done, t + 1)
                nc.scalar.activation(h1[:, :], mlp_ps[:, 0:H1], ACT.Relu).then_inc(h1_ready, 1)

            def tile(t, first):
                for p in range(1, TP, 2):
                    if not first and p == SP + 1:
                        relu_h1(t - 1)
                    copy_pair(t, p, first)
                    s, q = p // SP - 1, 2 + p % SP // 2
                    if s >= 0:
                        copy_dots(t, s, q, first)
                    elif not first:
                        copy_dots(t - 1, TS - 1, q, False)

            act.dma_start(base[:, :], table_base).then_inc(base_loaded, 16)
            tile(0, True)
            with act.Fori(1, NT) as t:
                tile(t, False)
            copy_dots(NT - 1, TS - 1, 2, False)
            copy_dots(NT - 1, TS - 1, 3, False)
            for c in range(2):
                act.wait_ge(half1_done, c + 1)
                nc.scalar.activation(h1[:, c * H1 // 2:(c + 1) * H1 // 2], half_ps[c],
                                     ACT.Relu).then_inc(half_h1_ready, 1)


def kernel(**inputs):
    import numpy as np
    import concourse.bacc as bacc
    from concourse import mybir as mb
    from concourse.bass_utils import run_bass_kernel_spmd as run

    tbls = [np.asarray(inputs[f"tbl_{f}"]) for f in range(NF)]
    ids = np.asarray(inputs["ids"])
    w1 = np.asarray(inputs["W_top1"])
    b = ids.shape[0]
    h1 = w1.shape[1]

    starts = np.cumsum([0] + [t.shape[0] for t in tbls])[:NF].astype(np.int32)

    w1_l = np.zeros((P // Q, Q, NJ, h1), w1.dtype)
    iu, ju = np.triu_indices(NF, k=1)
    w1_l[ju // NJ, iu, ju % NJ] = w1[:iu.size]
    dense = w1.shape[0] - iu.size
    w1_l[0, :dense, 0] = w1[iu.size:]
    w1_l[0, dense, 0] = np.asarray(inputs["b_top1"])

    arrays = {
        "tables": np.concatenate(tbls, axis=0),
        "idx": np.ascontiguousarray(ids.reshape(b // GB, GB * NF).T),
        "table_base": np.tile(starts, GB).reshape(P, 1),
        "dense_t": np.ascontiguousarray(np.asarray(inputs["dense_ctx"]).T),
        "w1": w1_l.reshape(P, NJ, h1),
        "w2": np.asarray(inputs["W_top2"]),
        "b2": np.asarray(inputs["b_top2"]).reshape(1, -1),
        "w3": np.asarray(inputs["W_top3"]).reshape(1, -1),
    }
    nc = bacc.Bacc("TRN2", target_bir_lowering=False, num_devices=1)
    args = [nc.dram_tensor(n, a.shape, mb.dt.from_np(a.dtype), kind="ExternalInput").ap()
            for n, a in arrays.items()]
    out = nc.dram_tensor("out", (b, 1), mb.dt.float32, kind="ExternalOutput").ap()
    dlrm_tower(nc, *args, out)
    r = run(nc, [arrays], core_ids=[0])
    return r.results[0]["out"]
```
